# Optimizing a Trainium2 kernel written in Bass

```python
import numpy as np
import jax
import jax.numpy as jnp

def _softmax(x, axis=-1):
    return jax.nn.softmax(x, axis=axis)

def _gelu(x):
    return jax.nn.gelu(x, approximate=True)

def _silu(x):
    return jax.nn.silu(x)

def _sigmoid(x):
    return jax.nn.sigmoid(x)

def _layernorm(x, axis=-1, eps=1e-05):
    m = jnp.mean(x, axis=axis, keepdims=True)
    v = jnp.var(x, axis=axis, keepdims=True)
    return (x - m) / jnp.sqrt(v + eps)

def _scatter_add(tgt, idx, src, axis=0):
    return tgt.at[idx].add(src)

def _segment_sum(src, seg, n):
    return jax.ops.segment_sum(src, seg, n)
kernel_name = 'mk_flamingo_gated_d1_seqx_r4_fb427b'

def setup_inputs(seed: int=0):
    np.random.seed(seed)
    _w = jnp.asarray

    def _rec_inputs():
        import jax
        import jax.numpy as jnp
        _rk = jax.random.key(seed)
        x = -0.0002928 + 1 * jax.random.normal(jax.random.fold_in(_rk, 1), (16, 256, 256), jnp.float32)
        _lenS = 256 - jax.random.randint(jax.random.fold_in(_rk, 7), (16,), 0, max(1, 256 // 4) + 1, jnp.int32)
        _lenS2 = 256 - jax.random.randint(jax.random.fold_in(_rk, 8), (16,), 0, max(1, 256 // 4) + 1, jnp.int32)
        _ctx_1024P = jax.random.normal(jax.random.fold_in(_rk, 11), (16, 16, 256), jnp.float32)
        _ctx_1024c = jax.random.dirichlet(jax.random.fold_in(_rk, 511), 0.3 * jnp.ones((16,), jnp.float32), (16, 256))
        _ctx_1024t = jnp.einsum('bsk,bkd->bsd', _ctx_1024c, _ctx_1024P)
        _ctx_1024t = _ctx_1024t * jax.lax.rsqrt(jnp.mean(jnp.square(_ctx_1024t)) + 1e-12) * 0.953939
        ctx_1024 = -1.39393e-06 + 0.999914 * (_ctx_1024t + 0.3 * jax.random.normal(jax.random.fold_in(_rk, 611), (16, 256, 256), jnp.float32))
        _g = jax.random.normal(jax.random.fold_in(_rk, 9001), (2, 1), jnp.float32)
        _g = jnp.sign(_g) * jnp.maximum(jnp.abs(_g), 1.0) + (_g == 0) * 1.0
        g_xattn = _g[0]
        g_ffn = _g[1]
        return (x, ctx_1024, g_xattn, g_ffn)
    x, ctx_1024, g_xattn, g_ffn = _rec_inputs()

    def _L0_xattn_setup():
        import jax, jax.numpy as jnp
        import numpy as np
        D_MODEL = 256
        N_HEADS = 16
        D_HEAD = D_MODEL // N_HEADS
        WINDOW = 128

        def _heads(x):
            B, S, _ = x.shape
            return x.reshape(B, S, N_HEADS, D_HEAD).transpose(0, 2, 1, 3)
        key = jax.random.key(seed)
        ks = jax.random.split(key, 11)
        B, S = (1, 1024)
        s = 1.0 / np.sqrt(D_MODEL)
        return {'query': jax.random.normal(ks[0], (B, S, D_MODEL), jnp.float32), 'key': jax.random.normal(ks[1], (B, S, D_MODEL), jnp.float32), 'value': jax.random.normal(ks[2], (B, S, D_MODEL), jnp.float32), 'Wq': jax.random.normal(ks[3], (D_MODEL, D_MODEL), jnp.float32) * s, 'bq': jnp.zeros((D_MODEL,), jnp.float32), 'Wk': jax.random.normal(ks[4], (D_MODEL, D_MODEL), jnp.float32) * s, 'bk': jnp.zeros((D_MODEL,), jnp.float32), 'Wv': jax.random.normal(ks[5], (D_MODEL, D_MODEL), jnp.float32) * s, 'bv': jnp.zeros((D_MODEL,), jnp.float32), 'Wo': jax.random.normal(ks[6], (D_MODEL, D_MODEL), jnp.float32) * s, 'bo': jnp.zeros((D_MODEL,), jnp.float32)}
    _L0_xattn_all = _L0_xattn_setup()
    _L0_xattn_in = {k: v for k, v in _L0_xattn_all.items() if k in ('Wq', 'bq', 'Wk', 'bk', 'Wv', 'bv', 'Wo', 'bo')}
    del _L0_xattn_all

    def _L0_ffn_setup():
        import jax, jax.numpy as jnp
        import numpy as np
        DIM = 256

        def _reference_tuple_inner(x, W_r, W_k, W_v, mu_r, mu_k):
            B, T, C = x.shape
            x_prev = jnp.concatenate([jnp.zeros((B, 1, C), x.dtype), x[:, :-1, :]], axis=1)
            xr = mu_r * x + (1.0 - mu_r) * x_prev
            xk = mu_k * x + (1.0 - mu_k) * x_prev
            r = jax.nn.sigmoid(jnp.einsum('btc,dc->btd', xr, W_r))
            k = jnp.einsum('btc,dc->btd', xk, W_k)
            k_act = jnp.square(jax.nn.relu(k))
            out = r * jnp.einsum('btc,dc->btd', k_act, W_v)
            new_state = x[:, -1, :]
            return (out, new_state)
        key = jax.random.key(seed)
        ks = jax.random.split(key, 6)
        B, T, C = (8, 512, DIM)
        x = jax.random.normal(ks[0], (B, T, C), dtype=jnp.float32)
        s = 1.0 / np.sqrt(C)
        W_r = jax.random.uniform(ks[1], (C, C), jnp.float32, -s, s)
        W_k = jax.random.uniform(ks[2], (C, C), jnp.float32, -s, s)
        W_v = jax.random.uniform(ks[3], (C, C), jnp.float32, -s, s)
        mu_r = jax.random.uniform(ks[4], (C,), jnp.float32)
        mu_k = jax.random.uniform(ks[5], (C,), jnp.float32)
        return {'x': x, 'W_r': W_r, 'W_k': W_k, 'W_v': W_v, 'mu_r': mu_r, 'mu_k': mu_k}
    _L0_ffn_all = _L0_ffn_setup()
    _L0_ffn_in = {k: v for k, v in _L0_ffn_all.items() if k in ('W_r', 'W_k', 'W_v', 'mu_r', 'mu_k')}
    del _L0_ffn_all
    return {'x': x, 'ctx_1024': ctx_1024, 'g_xattn': g_xattn, 'g_ffn': g_ffn, 'L0_xattn_Wq': _L0_xattn_in['Wq'], 'L0_xattn_bq': _L0_xattn_in['bq'], 'L0_xattn_Wk': _L0_xattn_in['Wk'], 'L0_xattn_bk': _L0_xattn_in['bk'], 'L0_xattn_Wv': _L0_xattn_in['Wv'], 'L0_xattn_bv': _L0_xattn_in['bv'], 'L0_xattn_Wo': _L0_xattn_in['Wo'], 'L0_xattn_bo': _L0_xattn_in['bo'], 'L0_ffn_W_r': _L0_ffn_in['W_r'], 'L0_ffn_W_k': _L0_ffn_in['W_k'], 'L0_ffn_W_v': _L0_ffn_in['W_v'], 'L0_ffn_mu_r': _L0_ffn_in['mu_r'], 'L0_ffn_mu_k': _L0_ffn_in['mu_k']}

def reference(x, ctx_1024, g_xattn, g_ffn, L0_xattn_Wq, L0_xattn_bq, L0_xattn_Wk, L0_xattn_bk, L0_xattn_Wv, L0_xattn_bv, L0_xattn_Wo, L0_xattn_bo, L0_ffn_W_r, L0_ffn_W_k, L0_ffn_W_v, L0_ffn_mu_r, L0_ffn_mu_k):
    import jax
    import jax.numpy as jnp

    def _L0_xattn_ref(query, key, value, Wq, bq, Wk, bk, Wv, bv, Wo, bo):
        import jax, jax.numpy as jnp
        import numpy as np
        D_MODEL = 256
        N_HEADS = 16
        D_HEAD = D_MODEL // N_HEADS
        WINDOW = 128

        def _heads(x):
            B, S, _ = x.shape
            return x.reshape(B, S, N_HEADS, D_HEAD).transpose(0, 2, 1, 3)
        B, S, _ = query.shape
        q = _heads(query @ Wq.T + bq)
        k = _heads(key @ Wk.T + bk)
        v = _heads(value @ Wv.T + bv)
        scores = jnp.einsum('bhqd,bhkd->bhqk', q, k) / np.sqrt(D_HEAD).astype(np.float32)
        idx = jnp.arange(S)
        local = jnp.abs(idx[:, None] - idx[None, :]) <= WINDOW // 2
        scores = jnp.where(local[None, None, :, :], scores, -jnp.inf)
        attn = jax.nn.softmax(scores, axis=-1)
        ctx = jnp.einsum('bhqk,bhkd->bhqd', attn, v)
        ctx = ctx.transpose(0, 2, 1, 3).reshape(B, S, D_MODEL)
        return ctx @ Wo.T + bo

    def _L0_ffn_ref(x, W_r, W_k, W_v, mu_r, mu_k):
        import jax, jax.numpy as jnp
        import numpy as np
        DIM = 256

        def _reference_tuple_inner(x, W_r, W_k, W_v, mu_r, mu_k):
            B, T, C = x.shape
            x_prev = jnp.concatenate([jnp.zeros((B, 1, C), x.dtype), x[:, :-1, :]], axis=1)
            xr = mu_r * x + (1.0 - mu_r) * x_prev
            xk = mu_k * x + (1.0 - mu_k) * x_prev
            r = jax.nn.sigmoid(jnp.einsum('btc,dc->btd', xr, W_r))
            k = jnp.einsum('btc,dc->btd', xk, W_k)
            k_act = jnp.square(jax.nn.relu(k))
            out = r * jnp.einsum('btc,dc->btd', k_act, W_v)
            new_state = x[:, -1, :]
            return (out, new_state)
        return _reference_tuple_inner(x, W_r, W_k, W_v, mu_r, mu_k)[0]
    x = x + jnp.tanh(g_xattn[0]) * _L0_xattn_ref(_layernorm(x, axis=-1), ctx_1024, ctx_1024, L0_xattn_Wq, L0_xattn_bq, L0_xattn_Wk, L0_xattn_bk, L0_xattn_Wv, L0_xattn_bv, L0_xattn_Wo, L0_xattn_bo)
    x = x + jnp.tanh(g_ffn[0]) * _L0_ffn_ref(_layernorm(x, axis=-1), L0_ffn_W_r, L0_ffn_W_k, L0_ffn_W_v, L0_ffn_mu_r, L0_ffn_mu_k)
    return x

_drawn_inputs = setup_inputs


def setup_inputs(seed=0):
    import zlib

    import numpy as np

    out = dict(_drawn_inputs(seed))
    spreads = {'L0_xattn_bq': (0.0, 0.467),
     'L0_xattn_bk': (0.0, 0.8),
     'L0_xattn_bv': (0.0, 0.1),
     'L0_xattn_bo': (0.0, 0.1)}
    factors = {'L0_ffn_W_r': 3.331, 'L0_ffn_mu_r': 7.48}
    for name, (base, spread) in spreads.items():
        noise = np.random.default_rng([zlib.crc32(name.encode()), seed]).standard_normal(out[name].shape)
        drawn = base * np.exp(spread * noise) if base else spread * noise
        out[name] = jnp.asarray(drawn.astype(out[name].dtype))
    for name, factor in factors.items():
        out[name] = (out[name] * factor).astype(out[name].dtype)
    return out
```

```python
import concourse.bass as bass
from concourse import mybir
from contextlib import ExitStack


def flamingo_block(nc, x, ctx_t, g_xattn, g_ffn, w_q, b_q, w_k, b_k, w_v, b_v, w_o, b_o,
                   w_r, w_kf, w_vf, mu_r, mu_k, out):
    F32, F32R, BF16 = mybir.dt.float32, mybir.dt.float32r, mybir.dt.bfloat16
    ALU, ACT, AX = mybir.AluOpType, mybir.ActivationFunctionType, mybir.AxisListType
    SP, PE = mybir.EngineType.SP, mybir.EngineType.PE
    DVE, ACTE, POOL = mybir.EngineType.DVE, mybir.EngineType.Activation, mybir.EngineType.Pool

    B, T, D = x.shape
    H = 16
    DH = D // H
    HALF = 64
    P = 128
    C = T // P
    FC = D // P
    GH = 4
    G = H // GH
    BAND = P + HALF
    UNITS = G * C
    PAD = P // GH
    SHIFT = 4 * DH
    MASKED = -3.0e38
    EPS = 1e-5
    LOOP_FROM, LOOP_TO = 5, B - 1
    LAST = B + 3

    x_v = x.rearrange("b (c p) d -> b p c d", p=P)
    ctx_v = ctx_t.rearrange("b (f p) t -> b p f t", p=P)
    out_v = out.rearrange("b (c p) d -> b p c d", p=P)
    q_scratch = nc.dram_tensor("q_scratch", [2, 2, D, T], F32, kind="Internal").ap()
    k_scratch = nc.dram_tensor("k_scratch", [2, 2, D, T], F32, kind="Internal").ap()

    es = ExitStack()
    with es:
        def sb(name, shape, dt=F32):
            return es.enter_context(nc.sbuf_tensor(name, shape, dt))

        def pairs(name, shape, dt=F32):
            return [sb(f"{name}{i}", shape, dt) for i in range(2)]

        def sem(name):
            return es.enter_context(nc.semaphore(name))

        W = {"k": w_k, "v": w_v, "q": w_q, "o": w_o, "r": w_r, "kf": w_kf, "vf": w_vf}
        NAMES = list(W)
        FIRST = NAMES[:3]
        w_hi = {n: sb(f"w_hi_{n}", [P, FC, D], F32R) for n in NAMES}
        w_lo = {n: sb(f"w_lo_{n}", [P, FC, D], F32R) for n in NAMES}
        cols = sb("cols", [P, 5, FC])
        bq_scaled = sb("bq_scaled", [P, FC])
        bo_row = sb("bo_row", [P, D])
        bo_gated = sb("bo_gated", [P, D])
        gates = sb("gates", [P, 2])
        gate = sb("gate", [P, 2])
        half_gate = sb("half_gate", [P, 1])
        ident = sb("ident", [P, P])
        ident_b = sb("ident_b", [P, P], BF16)
        mask_f = sb("mask_f", [P, C, 2, BAND])
        mask_b = sb("mask_b", [P, C, 2 * BAND], BF16)
        neg_half = sb("neg_half", [P, C])
        q_tail = sb("q_tail", [P - SHIFT, 1, T])
        k_tail = sb("k_tail", [P - SHIFT, 1, T])

        x_in = pairs("x_in", [P, C, D])
        ctx_in = pairs("ctx_in", [P, FC, T])
        stats1, mv1, rstd1 = sb("stats1", [P, C, 6]), sb("mv1", [P, C, 2]), sb("rstd1", [P, C])
        var1 = sb("var1", [P, C])
        xn = sb("xn", [P, C, D])
        xnt_hi, xnt_lo = sb("xnt_hi", [P, FC, T], F32R), sb("xnt_lo", [P, FC, T], F32R)
        ctx_hi, ctx_lo = sb("ctx_hi", [P, FC, T], F32R), sb("ctx_lo", [P, FC, T], F32R)
        q_parts = sb("q_parts", [P, 2, FC, T], F32R)
        k_parts = sb("k_parts", [P, 2, FC, T], F32R)
        q_stack = pairs("q_stack", [P, H, T], F32R)
        k_stack = pairs("k_stack", [P, H, T], F32R)
        v_aug = pairs("v_aug", [P, C, H, PAD])
        row_max = pairs("row_max", [P, G, GH, C])
        neg_max = sb("neg_max", [GH * C, G, 2, P], F32R)
        probs = [sb(f"probs{i}", [P, GH, BAND]) for i in range(4)]
        heads_t = sb("heads_t", [P, G, T])
        inv_sum = sb("inv_sum", [P, C, H])
        heads = sb("heads", [P, C, D])
        att_hi, att_lo = sb("att_hi", [P, FC, T], F32R), sb("att_lo", [P, FC, T], F32R)
        x_res = sb("x_res", [P, C, D])
        x_bias = sb("x_bias", [P, C, D])
        x2 = pairs("x2", [P, C, D])
        stats2, mv2, rstd2 = sb("stats2", [P, C, 6]), sb("mv2", [P, C, 2]), sb("rstd2", [P, C])
        var2 = sb("var2", [P, C])
        x2n = sb("x2n", [P, C, D])
        x2t = sb("x2t", [P, FC, T + 1])
        step = sb("step", [P, FC, T])
        mr, mk = sb("mr", [P, FC, T]), sb("mk", [P, FC, T])
        mr_hi, mr_lo = sb("mr_hi", [P, FC, T], F32R), sb("mr_lo", [P, FC, T], F32R)
        mk_hi, mk_lo = sb("mk_hi", [P, FC, T], F32R), sb("mk_lo", [P, FC, T], F32R)
        gate_r = sb("gate_r", [P, C, D])
        k_relu, k_sq = sb("k_relu", [P, FC, T]), sb("k_sq", [P, FC, T])
        ka_hi, ka_lo = sb("ka_hi", [P, FC, T], F32R), sb("ka_lo", [P, FC, T], F32R)
        y = sb("y", [P, C, D])
        result = sb("result", [P, C, D])
        w_raw = dict(zip(NAMES, (x_res, x_bias, x2[0], x2[1], mr, mk, k_sq)))

        ps_scores = es.enter_context(nc.psum_tensor("ps_scores", [P, 2, 512], F32))
        ps_probs = es.enter_context(nc.psum_tensor("ps_probs", [P, 2, 512], F32))
        ps_pv = es.enter_context(nc.psum_tensor("ps_pv", [P, 512], F32))
        bank_x = es.enter_context(nc.psum_tensor("bank_x", [P, 512], F32))
        bank_y = es.enter_context(nc.psum_tensor("bank_y", [P, 512], F32))
        bank_z = es.enter_context(nc.psum_tensor("bank_z", [P, 512], F32))

        first_in, weights_in, small_in = sem("first_in"), sem("weights_in"), sem("small_in")
        gates_done, ident_done, const_done = sem("gates_done"), sem("ident_done"), sem("const_done")
        w_scaled, w_hi_done, w_lo_done = sem("w_scaled"), sem("w_hi_done"), sem("w_lo_done")
        mask_done, bias_done = sem("mask_done"), sem("bias_done")
        tails_set = [sem(f"tails_set{p}") for p in range(2)]
        dve_settled, pool_settled = sem("dve_settled"), sem("pool_settled")
        x_loaded, ctx_loaded, res_loaded = sem("x_loaded"), sem("ctx_loaded"), sem("res_loaded")
        q_spilled, k_spilled = sem("q_spilled"), sem("k_spilled")
        q_stacked, k_stacked, stored = sem("q_stacked"), sem("k_stacked"), sem("stored")
        max_placed = [sem(f"max_placed{g}") for g in range(G)]
        (stats1_done, mv1_done, var1_done, rstd1_done, xn_done, xnt_ready, xnt_hi_done,
         xnt_lo_done) = (sem(n) for n in ("stats1_done", "mv1_done", "var1_done", "rstd1_done",
                                          "xn_done", "xnt_ready", "xnt_hi_done", "xnt_lo_done"))
        ctx_hi_done, ctx_lo_done = sem("ctx_hi_done"), sem("ctx_lo_done")
        q_ready, q_hi_done, q_lo_done = sem("q_ready"), sem("q_hi_done"), sem("q_lo_done")
        k_ready, k_hi_done, k_lo_done = sem("k_ready"), sem("k_hi_done"), sem("k_lo_done")
        v_ready, v_done = sem("v_ready"), sem("v_done")
        scores_ready = [sem(f"scores_ready{u}") for u in range(UNITS)]
        max_done = [sem(f"max_done{u}") for u in range(UNITS)]
        maxt_ready = [sem(f"maxt_ready{g}") for g in range(G)]
        maxt_hi_done = [sem(f"maxt_hi_done{g}") for g in range(G)]
        maxt_lo_done = [sem(f"maxt_lo_done{g}") for g in range(G)]
        shifted_ready = [sem(f"shifted_ready{u}") for u in range(UNITS)]
        exp_done = [sem(f"exp_done{u}") for u in range(UNITS)]
        band_done = [sem(f"band_done{u}") for u in range(UNITS)]
        pv_done = [sem(f"pv_done{u}") for u in range(UNITS)]
        pv_out = [sem(f"pv_out{g}") for g in range(G)]
        heads_ready = [sem(f"heads_ready{c}") for c in range(C)]
        inv_done = [sem(f"inv_done{c}") for c in range(C)]
        heads_done = [sem(f"heads_done{c}") for c in range(C)]
        att_ready, att_hi_done, att_lo_done = sem("att_ready"), sem("att_hi_done"), sem("att_lo_done")
        bias_added, o_ready, x2_done = sem("bias_added"), sem("o_ready"), sem("x2_done")
        stats2_done, mv2_done, var2_done = sem("stats2_done"), sem("mv2_done"), sem("var2_done")
        rstd2_done, x2n_done = sem("rstd2_done"), sem("x2n_done")
        x2t_ready, x2t_done, step_done = sem("x2t_ready"), sem("x2t_done"), sem("step_done")
        mr_done, mk_done = sem("mr_done"), sem("mk_done")
        mr_hi_done, mr_lo_done = sem("mr_hi_done"), sem("mr_lo_done")
        mk_hi_done, mk_lo_done = sem("mk_hi_done"), sem("mk_lo_done")
        r_ready, r_done = sem("r_ready"), sem("r_done")
        kf_ready, k_relu_done, k_sq_done = sem("kf_ready"), sem("k_relu_done"), sem("k_sq_done")
        ka_hi_done, ka_lo_done = sem("ka_hi_done"), sem("ka_lo_done")
        vf_ready, y_done, result_done = sem("vf_ready"), sem("y_done"), sem("result_done")

        def wait(eng, s, b, per_batch=1):
            if not isinstance(b, int):
                eng.wait_ge(s, b * per_batch + per_batch)
            elif b >= 0:
                eng.wait_ge(s, (min(b, B - 1) + 1) * per_batch)

        def settle(eng, s):
            eng.sem_inc(s, 1)

        def at(a, b):
            return a[b] if isinstance(b, int) else a[bass.ds(b, 1)].rearrange("o p c d -> (o p) c d")

        def run(eng, iteration):
            for i in range(LOOP_FROM):
                iteration(i, i % 2)
            with eng.Fori(LOOP_FROM, LOOP_TO - 1, 2) as i:
                iteration(i, LOOP_FROM % 2)
                iteration(i + 1, (LOOP_FROM + 1) % 2)
            for i in range(LOOP_TO, LAST):
                iteration(i, i % 2)

        def has(b):
            return not isinstance(b, int) or 0 <= b < B

        def probs_unit(i, slot):
            return (slot + UNITS // 2) % UNITS, (i - 1 if slot >= UNITS // 2 else i - 2)

        def pv_unit(i, slot):
            return probs_unit(i, slot - 1) if slot else probs_unit(i - 1, UNITS - 1)

        block = es.enter_context(nc.Block())

        @block.sync
        def _(sp):
            for n, col in enumerate((b_q, b_k, b_v, mu_r, mu_k)):
                sp.dma_start(cols[:, n, :], col).then_inc(small_in, 16)
            sp.dma_start(gates[:, 0:1], g_xattn.to_broadcast([P, 1])).then_inc(small_in, 16)
            sp.dma_start(gates[:, 1:2], g_ffn.to_broadcast([P, 1])).then_inc(small_in, 16)
            sp.dma_start(bo_row[:], b_o.to_broadcast([P, D])).then_inc(small_in, 16)

            def load_x(b, p):
                wait(sp, xn_done, b - 2)
                if isinstance(b, int) and b == 1:
                    sp.wait_ge(stats1_done, 1)
                sp.dma_start(x_in[p][:], at(x_v, b)).then_inc(x_loaded, 16)

            def load_ctx(b, p):
                wait(sp, ctx_lo_done, b - 2)
                if isinstance(b, int) and b == 1:
                    sp.wait_ge(ctx_hi_done, 1)
                sp.dma_start(ctx_in[p][:], at(ctx_v, b)).then_inc(ctx_loaded, 16)

            load_x(0, 0)
            load_ctx(0, 0)
            for n in NAMES:
                sp.dma_start(w_raw[n][:], W[n].rearrange("(f p) d -> p f d", p=P)
                             ).then_inc(first_in if n in FIRST else weights_in, 16)
            sp.wait_ge(const_done, 2)

            def set_tails(p):
                for stack, tail in ((q_stack, q_tail), (k_stack, k_tail)):
                    sp.dma_start(stack[p][SHIFT:P, :, :].bitcast(F32),
                                 tail[:].to_broadcast([P - SHIFT, H, T])).then_inc(tails_set[p], 16)

            set_tails(0)

            def spill_k(b, p):
                wait(sp, k_lo_done, b)
                wait(sp, k_stacked, b - 2, 64)
                sp.dma_start(k_scratch[p].rearrange("s (f r) t -> r s f t", f=FC),
                             k_parts[:].bitcast(F32)).then_inc(k_spilled, 16)

            def stack_k(b, p):
                wait(sp, k_spilled, b, 16)
                wait(sp, shifted_ready[UNITS - 1], b - 2)
                for n, part in enumerate((0, 0, 1, 1)):
                    sp.dma_start(k_stack[p][DH * n:DH * n + DH, :, :].bitcast(F32),
                                 k_scratch[p, part].rearrange("(h d) t -> d h t", d=DH)
                                 ).then_inc(k_stacked, 16)

            def spill_q(b, p):
                wait(sp, q_lo_done, b)
                wait(sp, q_stacked, b - 2, 80)
                sp.dma_start(q_scratch[p].rearrange("s (f r) t -> r s f t", f=FC),
                             q_parts[:].bitcast(F32)).then_inc(q_spilled, 16)

            def stack_q(b, p):
                wait(sp, q_spilled, b, 16)
                wait(sp, shifted_ready[UNITS - 1], b - 2)
                for n, part in enumerate((0, 1, 0, 1)):
                    sp.dma_start(q_stack[p][DH * n:DH * n + DH, :, :].bitcast(F32),
                                 q_scratch[p, part].rearrange("(h d) t -> d h t", d=DH)
                                 ).then_inc(q_stacked, 16)
                sp.dma_start(q_stack[p][SHIFT:SHIFT + 2, :, :].bitcast(F32),
                             q_tail[0:2, :, :].to_broadcast([2, H, T])).then_inc(q_stacked, 16)

            def place_max(b, p, g):
                wait(sp, maxt_lo_done[g], b)
                for part in range(2):
                    sp.dma_start(q_stack[p][SHIFT + part:SHIFT + part + 1, GH * g:GH * g + GH, :]
                                 .rearrange("o h (c t) -> o (h c) t", c=C).bitcast(F32),
                                 neg_max[:, g, part, :].bitcast(F32)).then_inc(max_placed[g], 16)

            def load_res(b):
                wait(sp, bias_added, b - 1)
                sp.dma_start(x_res[:], at(x_v, b)).then_inc(res_loaded, 16)

            def store(b):
                wait(sp, result_done, b)
                sp.dma_start(at(out_v, b), result[:]).then_inc(stored, 16)

            def iteration(i, p):
                if isinstance(i, int) and i == 2:
                    sp.wait_ge(w_lo_done, len(NAMES))
                if has(i - 2):
                    place_max(i - 2, p, 3)
                if has(i + 1):
                    load_x(i + 1, 1 - p)
                if has(i - 2):
                    load_res(i - 2)
                if has(i - 1):
                    place_max(i - 1, 1 - p, 0)
                if has(i):
                    spill_k(i, p)
                if has(i - 1):
                    place_max(i - 1, 1 - p, 1)
                if isinstance(i, int) and i < 2:
                    sp.wait_ge(tails_set[i], 32)
                if has(i):
                    spill_q(i, p)
                    stack_k(i, p)
                    stack_q(i, p)
                if isinstance(i, int) and i == 0:
                    set_tails(1)
                if has(i + 1):
                    load_ctx(i + 1, 1 - p)
                if has(i - 1):
                    place_max(i - 1, 1 - p, 2)
                if has(i - 3):
                    store(i - 3)

            run(sp, iteration)
            sp.wait_ge(stored, 16 * B)

        @block.tensor
        def _(pe):
            def product(dst, lhs, rhs, n):
                terms = [(l, r, f) for l, r in ((0, 0), (1, 0), (0, 1)) for f in range(n)]
                for k, (l, r, f) in enumerate(terms):
                    last = nc.tensor.matmul(dst, lhs(l, f), rhs(r, f), start=(k == 0),
                                            stop=(k == len(terms) - 1))
                return last

            def natural(bank, acts, w):
                for c in range(C):
                    last = product(bank[:, c * D:(c + 1) * D],
                                   lambda l, f: acts[l][:, f, c * P:(c + 1) * P],
                                   lambda r, f: (w_hi, w_lo)[r][w][:, f, :], FC)
                return last

            def transposed(bank, acts, w):
                for o in range(FC):
                    last = product(bank[:, o * T:(o + 1) * T],
                                   lambda l, f: (w_hi, w_lo)[l][w][:, f, o * P:(o + 1) * P],
                                   lambda r, f: acts[r][:, f, :], FC)
                return last

            def transpose_tokens(bank, src):
                for f in range(FC):
                    for c in range(C):
                        last = nc.tensor.transpose(bank[:, f * T + c * P:f * T + (c + 1) * P],
                                                   src[:, c, f * P:(f + 1) * P], ident[:])
                return last

            def scores(b, p, u):
                g, c = divmod(u, C)
                if u == 0:
                    wait(pe, k_stacked, b, 64)
                    wait(pe, q_stacked, b, 80)
                    wait(pe, max_done[UNITS - 1], b - 1)
                else:
                    wait(pe, max_done[u - 1], b)
                for j in range(GH):
                    h = GH * g + j
                    if j % 2 == 0:
                        nc.tensor.matmul(ps_scores[:, j // 2, 0:2 * BAND], ident_b[:], mask_b[:, c, :],
                                         start=True, stop=False, skip_group_check=True)
                    at_j = (j % 2) * BAND
                    last = nc.tensor.matmul(ps_scores[:, j // 2, at_j:at_j + BAND],
                                            q_stack[p][:, h, c * P:(c + 1) * P],
                                            k_stack[p][:, h, c * HALF:c * HALF + BAND],
                                            start=False, stop=True, skip_group_check=True)
                last.then_inc(scores_ready[u], 1)

            def shifted(b, p, u):
                g, c = divmod(u, C)
                wait(pe, max_placed[g], b, 32)
                if u == 0:
                    wait(pe, exp_done[UNITS - 1], b - 1)
                else:
                    wait(pe, exp_done[u - 1], b)
                for j in range(GH):
                    h = GH * g + j
                    at_j = (j % 2) * BAND
                    last = nc.tensor.matmul(ps_probs[:, j // 2, at_j:at_j + BAND],
                                            k_stack[p][:, h, c * P:(c + 1) * P],
                                            q_stack[p][:, h, c * HALF:c * HALF + BAND],
                                            start=True, stop=True)
                last.then_inc(shifted_ready[u], 1)

            def max_transpose(b, p, g, bank):
                wait(pe, max_done[C * g + C - 1], b)
                nc.tensor.transpose(bank[0:GH * C, 0:P],
                                    row_max[p][:, g, :, :].rearrange("q h c -> q (h c)"),
                                    ident[:]).then_inc(maxt_ready[g], 1)

            def pv(b, p, u):
                g, c = divmod(u, C)
                wait(pe, band_done[u], b)
                if u == 0:
                    wait(pe, v_done, b)
                if c == 0:
                    if g:
                        wait(pe, pv_out[g - 1], b)
                    else:
                        wait(pe, pv_out[G - 1], b - 1)
                for j in range(GH):
                    last = nc.tensor.matmul(ps_pv[PAD * j:PAD * (j + 1), c * HALF:c * HALF + BAND],
                                            v_aug[p][:, c, GH * g + j, :], probs[u % 4][:, j, :],
                                            start=(c == 0), stop=(c == C - 1), skip_group_check=True,
                                            tile_position=(0, PAD * j))
                last.then_inc(pv_done[u], 1)

            def iteration(i, p):
                a, b1, b2, b3 = i, i - 1, i - 2, i - 3
                if isinstance(i, int) and i == 2:
                    pe.wait_ge(w_lo_done, len(NAMES))
                for slot in range(UNITS):
                    if has(b1):
                        scores(b1, 1 - p, slot)
                    u, bu = probs_unit(i, slot)
                    if has(bu):
                        shifted(bu, p if slot < UNITS // 2 else 1 - p, u)
                    if slot == 0 and has(b2):
                        wait(pe, att_lo_done, b2 - 1)
                        max_transpose(b2, p, 3, bank_y)
                    if slot == 0 and has(b1):
                        wait(pe, y_done, b3 - 1)
                        natural(bank_x, (ctx_hi, ctx_lo), "v").then_inc(v_ready, 1)
                    if slot == 1 and has(b3):
                        wait(pe, x2n_done, b3)
                        wait(pe, maxt_lo_done[3], b2)
                        transpose_tokens(bank_y, x2n).then_inc(x2t_ready, 1)
                    if slot == 2 and has(b1):
                        wait(pe, x2_done, b3)
                        max_transpose(b1, 1 - p, 0, bank_z)
                    if slot == 2 and has(a):
                        wait(pe, xn_done, a)
                        wait(pe, v_done, b1)
                        transpose_tokens(bank_x, xn).then_inc(xnt_ready, 1)
                    if slot == 3 and has(a):
                        wait(pe, ctx_lo_done, a)
                        wait(pe, xnt_lo_done, a)
                        transposed(bank_x, (ctx_hi, ctx_lo), "k").then_inc(k_ready, 1)
                    if slot == 4 and has(b1):
                        wait(pe, maxt_lo_done[0], b1)
                        max_transpose(b1, 1 - p, 1, bank_z)
                    if slot == 4 and has(b3):
                        wait(pe, mr_lo_done, b3)
                        wait(pe, x2t_done, b3)
                        natural(bank_y, (mr_hi, mr_lo), "r").then_inc(r_ready, 1)
                    if slot == 4 and has(a):
                        wait(pe, k_lo_done, a)
                        transposed(bank_x, (xnt_hi, xnt_lo), "q").then_inc(q_ready, 1)
                    if slot == 5 and has(b3):
                        wait(pe, mk_lo_done, b3)
                        wait(pe, q_lo_done, a)
                        transposed(bank_x, (mk_hi, mk_lo), "kf").then_inc(kf_ready, 1)
                    if slot == 5 and has(b2):
                        wait(pe, pv_out[G - 1], b2)
                        wait(pe, r_done, b3)
                        wait(pe, maxt_lo_done[1], b1)
                        for c, bank in enumerate((bank_y, bank_z)):
                            for g in range(G):
                                last = nc.tensor.transpose(bank[:, g * P:(g + 1) * P],
                                                           heads_t[:, g, c * P:(c + 1) * P], ident[:])
                            last.then_inc(heads_ready[c], 1)
                    if slot == 6 and has(b1):
                        wait(pe, k_relu_done, b3)
                        max_transpose(b1, 1 - p, 2, bank_x)
                    if slot == 6 and has(b2):
                        wait(pe, heads_done[1], b2)
                        transpose_tokens(bank_y, heads).then_inc(att_ready, 1)
                    if slot == 7 and has(b2):
                        wait(pe, att_lo_done, b2)
                        natural(bank_z, (att_hi, att_lo), "o").then_inc(o_ready, 1)
                    if slot == 7 and has(b3):
                        wait(pe, ka_lo_done, b3)
                        wait(pe, maxt_lo_done[2], b1)
                        natural(bank_x, (ka_hi, ka_lo), "vf").then_inc(vf_ready, 1)
                    u, bu = pv_unit(i, slot)
                    if has(bu):
                        pv(bu, p if slot <= UNITS // 2 else 1 - p, u)

            pe.wait_ge(ident_done, 3)
            pe.wait_ge(mask_done, 3)
            pe.wait_ge(w_lo_done, 3)
            run(pe, iteration)

        @block.scalar
        def _(act):
            act.wait_ge(small_in, 16 * 8)
            nc.scalar.activation(gate[:], gates[:], ACT.Tanh).then_inc(gates_done, 1)

            def split_ctx(b, p):
                wait(act, ctx_loaded, b, 16)
                wait(act, v_ready, b - 1)
                nc.scalar.activation(ctx_hi[:], ctx_in[p][:], ACT.Copy).then_inc(ctx_hi_done, 1)

            def hi(src, dst, bias, ready, used, done, b):
                wait(act, ready, b)
                wait(act, used[0], b - 1, used[1])
                for f in range(FC):
                    last = nc.scalar.activation(dst[:, f, :], src[:, f * T:(f + 1) * T],
                                                ACT.Identity, bias=bias[:, f:f + 1])
                last.then_inc(done, 1)

            def exponent(b, u):
                wait(act, shifted_ready[u], b)
                if u >= 4:
                    wait(act, pv_done[u - 4], b)
                else:
                    wait(act, pv_done[u + 4], b - 1)
                nc.scalar.activation(probs[u % 4][:].rearrange("p (a e) q -> p a (e q)", a=2),
                                     ps_probs[:, :, 0:2 * BAND], ACT.Exp).then_inc(exp_done[u], 1)

            def max_hi(b, g, bank):
                wait(act, maxt_ready[g], b)
                wait(act, max_placed[g], b - 1, 32)
                nc.scalar.activation(neg_max[:, g, 0, :], bank[0:GH * C, 0:P], ACT.Copy,
                                     scale=-1.0).then_inc(maxt_hi_done[g], 1)

            def iteration(i, p):
                a, b1, b2, b3 = i, i - 1, i - 2, i - 3
                if isinstance(i, int) and i == 2:
                    act.wait_ge(w_lo_done, len(NAMES))
                for slot in range(UNITS):
                    u, bu = probs_unit(i, slot)
                    if has(bu):
                        exponent(bu, u)
                    if slot == 0 and has(b2):
                        max_hi(b2, 3, bank_y)
                    if slot == 0 and has(b1):
                        wait(act, v_ready, b1)
                        wait(act, pv_done[UNITS - 1], b1 - 2)
                        nc.scalar.activation(v_aug[1 - p][:, :, :, 0:DH],
                                             bank_x[:].rearrange("p (c h d) -> p c h d", c=C, h=H),
                                             ACT.Copy).then_inc(v_done, 1)
                    if slot == 1 and has(a):
                        split_ctx(a, p)
                    if slot == 1 and has(b3):
                        wait(act, x2t_ready, b3)
                        wait(act, mk_done, b3 - 1)
                        nc.scalar.activation(x2t[:, :, 1:T + 1],
                                             bank_y[:].rearrange("p (f t) -> p f t", f=FC),
                                             ACT.Copy).then_inc(x2t_done, 1)
                    if slot == 2 and has(b1):
                        max_hi(b1, 0, bank_z)
                    if slot == 2 and has(a):
                        wait(act, xnt_ready, a)
                        wait(act, q_ready, a - 1)
                        nc.scalar.activation(xnt_hi[:].rearrange("p f t -> p (f t)"), bank_x[:],
                                             ACT.Copy).then_inc(xnt_hi_done, 1)
                    if slot == 3 and has(a):
                        hi(bank_x, k_parts[:, 0], cols[:, 1, :], k_ready, (k_spilled, 16),
                           k_hi_done, a)
                    if slot == 4 and has(b1):
                        max_hi(b1, 1, bank_z)
                    if slot == 4 and has(b3):
                        wait(act, r_ready, b3)
                        wait(act, y_done, b3 - 1)
                        nc.scalar.activation(gate_r[:].rearrange("p c d -> p (c d)"), bank_y[:],
                                             ACT.Tanh, scale=0.5).then_inc(r_done, 1)
                    if slot == 4 and has(a):
                        hi(bank_x, q_parts[:, 0], bq_scaled, q_ready, (q_spilled, 16), q_hi_done, a)
                    if slot == 5 and has(b3):
                        wait(act, kf_ready, b3)
                        wait(act, k_sq_done, b3 - 1)
                        nc.scalar.activation(k_relu[:].rearrange("p f t -> p (f t)"), bank_x[:],
                                             ACT.Relu).then_inc(k_relu_done, 1)
                    if slot == 6 and has(b1):
                        max_hi(b1, 2, bank_x)
                    if slot == 6 and has(b2):
                        hi(bank_y, att_hi, cols[:, 2, :], att_ready, (o_ready, 1), att_hi_done, b2)
                    u, bu = pv_unit(i, slot)
                    if has(bu) and u % C == C - 1:
                        g = u // C
                        wait(act, pv_done[u], bu)
                        if g == 0:
                            wait(act, heads_ready[1], bu - 1)
                        nc.scalar.activation(heads_t[:, g, :], ps_pv[:, 0:T],
                                             ACT.Copy).then_inc(pv_out[g], 1)

            act.wait_ge(const_done, 2)
            act.wait_ge(bias_done, 1)
            run(act, iteration)

        @block.vector
        def _(dve):
            dve.wait_ge(small_in, 16 * 8)
            nc.vector.tensor_scalar(bq_scaled[:], cols[:, 0, :], DH ** -0.5, None,
                                    ALU.mult).then_inc(bias_done, 1)

            def split_weights(names, first):
                for n, name in enumerate(names):
                    nc.vector.tensor_copy(w_hi[name][:], w_raw[name][:]).then_inc(w_hi_done, 1)
                for n, name in enumerate(names):
                    dve.wait_ge(w_hi_done, first + n + 1)
                    nc.vector.tensor_tensor(w_lo[name][:], w_raw[name][:], w_hi[name][:],
                                            ALU.subtract).then_inc(w_lo_done, 1)

            def first_weights():
                dve.wait_ge(first_in, 16 * len(FIRST))
                nc.vector.tensor_scalar(w_raw["q"][:], w_raw["q"][:], DH ** -0.5, None,
                                        ALU.mult).then_inc(w_scaled, 1)
                dve.wait_ge(w_scaled, 1)
                split_weights(FIRST, 0)

            def other_weights():
                dve.wait_ge(gates_done, 1)
                nc.vector.tensor_scalar(bo_gated[:], bo_row[:], gate[:, 0:1], None,
                                        ALU.mult).then_inc(bias_done, 1)
                nc.vector.tensor_scalar(half_gate[:], gate[:, 1:2], 0.5, None,
                                        ALU.mult).then_inc(bias_done, 1)
                dve.wait_ge(weights_in, 16 * (len(NAMES) - len(FIRST)))
                dve.wait_ge(bias_done, 3)
                nc.vector.tensor_scalar(w_raw["o"][:], w_raw["o"][:], gate[:, 0:1], None, ALU.mult)
                nc.vector.tensor_scalar(w_raw["vf"][:], w_raw["vf"][:], half_gate[:], None,
                                        ALU.mult).then_inc(w_scaled, 1)
                dve.wait_ge(w_scaled, 2)
                split_weights(NAMES[len(FIRST):], len(FIRST))

            def statistics(src, stats, mv, stats_sem, mv_sem, b):
                for c in range(C):
                    last = nc.vector.bn_stats(stats[:, c, :], src[:, c, :])
                last.then_inc(stats_sem, 1)
                wait(dve, stats_sem, b)
                settle(dve, dve_settled)
                for c in range(C):
                    last = nc.vector.bn_aggr(mv[:, c, :], stats[:, c:c + 1, :])
                last.then_inc(mv_sem, 1)

            def normalise(dst, src, mv, rstd):
                for c in range(C):
                    last = nc.vector.tensor_scalar(dst[:, c, :], src[:, c, :], mv[:, c, 0:1],
                                                   rstd[:, c:c + 1], ALU.subtract, ALU.mult)
                return last

            def lo(src, hi_part, dst, bias, done, b):
                for f in range(FC):
                    last = nc.vector.scalar_tensor_tensor(
                        out=dst[:, f, :], in0=src[:, f * T:(f + 1) * T], scalar=bias[:, f:f + 1],
                        in1=hi_part[:, f, :], op0=ALU.add, op1=ALU.subtract)
                last.then_inc(done, 1)

            def maxima(b, p, u):
                g, c = divmod(u, C)
                wait(dve, scores_ready[u], b)
                if u % C == 0:
                    wait(dve, maxt_ready[g], b - 2)
                nc.vector.tensor_reduce(
                    row_max[p][:, g, :, c].rearrange("q (a e) -> q a e", a=2),
                    ps_scores[:, :, 0:2 * BAND].rearrange("q a (e k) -> q a e k", e=2),
                    AX.X, ALU.max).then_inc(max_done[u], 1)

            def max_lo(b, g, bank):
                wait(dve, maxt_hi_done[g], b)
                nc.vector.scalar_tensor_tensor(
                    out=neg_max[:, g, 1, :], in0=bank[0:GH * C, 0:P], scalar=-1.0,
                    in1=neg_max[:, g, 0, :], op0=ALU.mult, op1=ALU.subtract
                ).then_inc(maxt_lo_done[g], 1)

            def iteration(i, p):
                a, b1, b2, b3 = i, i - 1, i - 2, i - 3
                if isinstance(i, int) and i == 2:
                    dve.wait_ge(w_lo_done, len(NAMES))
                for slot in range(UNITS):
                    if has(b1):
                        maxima(b1, 1 - p, slot)
                    if slot == 0 and has(b3):
                        wait(dve, rstd2_done, b3)
                        wait(dve, x2t_ready, b3 - 1)
                        normalise(x2n, x2[1 - p], mv2, rstd2).then_inc(x2n_done, 1)
                    if slot == 0 and has(b2):
                        max_lo(b2, 3, bank_y)
                    if slot == 0 and has(a):
                        wait(dve, x_loaded, a, 16)
                        wait(dve, xn_done, a - 1)
                        wait(dve, var1_done, a - 1)
                        statistics(x_in[p], stats1, mv1, stats1_done, mv1_done, a)
                    if slot == 1 and has(a):
                        wait(dve, rstd1_done, a)
                        wait(dve, xnt_ready, a - 1)
                        normalise(xn, x_in[p], mv1, rstd1).then_inc(xn_done, 1)
                    if isinstance(i, int) and (i, slot) == (0, 1):
                        first_weights()
                    if isinstance(i, int) and (i, slot) == (0, 7):
                        other_weights()
                    if slot == 2 and has(b1):
                        max_lo(b1, 0, bank_z)
                    if slot == 2 and has(a):
                        wait(dve, xnt_hi_done, a)
                        nc.vector.tensor_tensor(xnt_lo[:].rearrange("p f t -> p (f t)"), bank_x[:],
                                                xnt_hi[:].rearrange("p f t -> p (f t)"),
                                                ALU.subtract).then_inc(xnt_lo_done, 1)
                    if slot == 2 and has(b3):
                        wait(dve, step_done, b3)
                        for dst, m, done, lo_done in ((mr, 3, mr_done, mr_lo_done),
                                                      (mk, 4, mk_done, mk_lo_done)):
                            wait(dve, lo_done, b3 - 1)
                            for f in range(FC):
                                last = nc.vector.scalar_tensor_tensor(
                                    out=dst[:, f, :], in0=step[:, f, :], scalar=cols[:, m, f:f + 1],
                                    in1=x2t[:, f, 0:T], op0=ALU.mult, op1=ALU.add)
                            last.then_inc(done, 1)
                        wait(dve, mr_done, b3)
                        wait(dve, r_ready, b3 - 1)
                        nc.vector.tensor_copy(mr_hi[:], mr[:]).then_inc(mr_hi_done, 1)
                    if slot == 3 and has(b3):
                        wait(dve, mk_done, b3)
                        wait(dve, kf_ready, b3 - 1)
                        nc.vector.tensor_copy(mk_hi[:], mk[:]).then_inc(mk_hi_done, 1)
                        wait(dve, mr_hi_done, b3)
                        nc.vector.tensor_tensor(mr_lo[:], mr[:], mr_hi[:],
                                                ALU.subtract).then_inc(mr_lo_done, 1)
                    if slot == 3 and has(a):
                        wait(dve, k_hi_done, a)
                        lo(bank_x, k_parts[:, 0], k_parts[:, 1], cols[:, 1, :], k_lo_done, a)
                    if slot == 4 and has(b1):
                        max_lo(b1, 1, bank_z)
                    if slot == 4 and has(a):
                        wait(dve, q_hi_done, a)
                        lo(bank_x, q_parts[:, 0], q_parts[:, 1], bq_scaled, q_lo_done, a)
                    if slot == 5 and has(b2):
                        for c, bank in enumerate((bank_y, bank_z)):
                            v = bank[:].rearrange("q (h r) -> q h r", h=H)
                            wait(dve, heads_ready[c], b2)
                            wait(dve, heads_done[c], b2 - 1)
                            wait(dve, att_ready, b2 - 1)
                            nc.vector.reciprocal(inv_sum[:, c, :], v[:, :, DH]).then_inc(inv_done[c], 1)
                            wait(dve, inv_done[c], b2)
                            nc.vector.tensor_tensor(
                                heads[:, c, :].rearrange("q (h d) -> q h d", h=H), v[:, :, 0:DH],
                                inv_sum[:, c, :].unsqueeze(2).to_broadcast([P, H, DH]),
                                ALU.mult).then_inc(heads_done[c], 1)
                    if slot == 6 and has(b1):
                        max_lo(b1, 2, bank_x)
                    if slot == 6 and has(b2):
                        wait(dve, att_hi_done, b2)
                        lo(bank_y, att_hi, att_lo, cols[:, 2, :], att_lo_done, b2)
                    if slot == 6 and has(b3):
                        wait(dve, k_sq_done, b3)
                        wait(dve, vf_ready, b3 - 1)
                        nc.vector.tensor_copy(ka_hi[:], k_sq[:]).then_inc(ka_hi_done, 1)
                        wait(dve, ka_hi_done, b3)
                        nc.vector.tensor_tensor(ka_lo[:], k_sq[:], ka_hi[:],
                                                ALU.subtract).then_inc(ka_lo_done, 1)
                    if slot == 7 and has(b2):
                        wait(dve, o_ready, b2)
                        wait(dve, bias_added, b2)
                        wait(dve, result_done, b2 - 2)
                        nc.vector.tensor_tensor(x2[p][:].rearrange("p c d -> p (c d)"), bank_z[:],
                                                x_bias[:].rearrange("p c d -> p (c d)"),
                                                ALU.add).then_inc(x2_done, 1)
                        wait(dve, x2_done, b2)
                        wait(dve, x2n_done, b2 - 1)
                        wait(dve, var2_done, b2 - 1)
                        statistics(x2[p], stats2, mv2, stats2_done, mv2_done, b2)
                    if slot == 7 and has(b3):
                        wait(dve, vf_ready, b3)
                        wait(dve, r_done, b3)
                        wait(dve, result_done, b3 - 1)
                        nc.vector.scalar_tensor_tensor(
                            out=y[:].rearrange("p c d -> p (c d)"),
                            in0=gate_r[:].rearrange("p c d -> p (c d)"), scalar=1.0, in1=bank_x[:],
                            op0=ALU.add, op1=ALU.mult).then_inc(y_done, 1)

            run(dve, iteration)

        @block.gpsimd
        def _(pool):
            nc.gpsimd.memset(ident[:], 0.0).then_inc(ident_done, 1)
            pool.wait_ge(ident_done, 1)
            nc.gpsimd.affine_select(out=ident[:], in_=ident[:], compare_op=ALU.not_equal, fill=1.0,
                                    base=0, pattern=[[-1, P]],
                                    channel_multiplier=1).then_inc(ident_done, 1)
            nc.gpsimd.memset(mask_f[:], 0.0).then_inc(mask_done, 1)

            def band(t, c, heads_, fill):
                first = HALF if c == 0 else P
                nc.gpsimd.affine_select(out=t[:, :, 0:first], in_=t[:, :, 0:first],
                                        compare_op=ALU.is_ge, fill=fill,
                                        base=HALF if c == 0 else 0, pattern=[[0, heads_], [1, first]],
                                        channel_multiplier=-1)
                return nc.gpsimd.affine_select(out=t[:, :, first:BAND], in_=t[:, :, first:BAND],
                                               compare_op=ALU.is_ge, fill=fill, base=0,
                                               pattern=[[0, heads_], [-1, BAND - first]],
                                               channel_multiplier=1)

            pool.wait_ge(mask_done, 1)
            band(mask_f[:, 0], 0, 2, MASKED)
            band(mask_f[:, 1], 1, 2, MASKED).then_inc(mask_done, 1)
            pool.wait_ge(ident_done, 2)
            pool.wait_ge(mask_done, 2)
            nc.gpsimd.tensor_copy(ident_b[:], ident[:]).then_inc(ident_done, 1)
            nc.gpsimd.tensor_copy(mask_b[:], mask_f[:].rearrange("p c e k -> p c (e k)")
                                  ).then_inc(mask_done, 1)
            nc.gpsimd.memset(neg_half[:], -0.5)
            nc.gpsimd.memset(x2t[:, :, 0:1], 0.0)
            nc.gpsimd.memset(q_tail[:], 0.0)
            nc.gpsimd.memset(v_aug[0][:, :, :, DH:PAD], 1.0)
            nc.gpsimd.memset(v_aug[1][:, :, :, DH:PAD], 1.0)
            nc.gpsimd.memset(k_tail[:], 0.0).then_inc(const_done, 1)
            pool.wait_ge(const_done, 1)
            nc.gpsimd.memset(k_tail[0:2, :, :], 1.0).then_inc(const_done, 1)

            def rstd(var, mv, dst, mv_sem, var_sem, rstd_sem, used, b):
                wait(pool, mv_sem, b)
                wait(pool, used, b - 1)
                settle(pool, pool_settled)
                nc.gpsimd.tensor_scalar(var[:], mv[:, :, 1], EPS, None, ALU.add).then_inc(var_sem, 1)
                wait(pool, var_sem, b)
                nc.gpsimd.tensor_tensor(dst[:], var[:], neg_half[:], ALU.pow).then_inc(rstd_sem, 1)

            def iteration(i, p):
                a, b1, b2, b3 = i, i - 1, i - 2, i - 3
                if isinstance(i, int) and i == 2:
                    pool.wait_ge(w_lo_done, len(NAMES))
                for slot in range(UNITS):
                    if slot == 6 and has(b3):
                        wait(pool, k_relu_done, b3)
                        wait(pool, ka_lo_done, b3 - 1)
                        nc.gpsimd.tensor_tensor(k_sq[:], k_relu[:], k_relu[:],
                                                ALU.mult).then_inc(k_sq_done, 1)
                    u, bu = probs_unit(i, slot)
                    if has(bu):
                        wait(pool, exp_done[u], bu)
                        settle(pool, pool_settled)
                        band(probs[u % 4], u % C, GH, 0.0).then_inc(band_done[u], 1)
                    if slot == 0 and has(a):
                        rstd(var1, mv1, rstd1, mv1_done, var1_done, rstd1_done, xn_done, a)
                    if slot == 1 and has(b3):
                        wait(pool, x2t_done, b3)
                        wait(pool, mk_done, b3 - 1)
                        nc.gpsimd.tensor_tensor(step[:], x2t[:, :, 1:T + 1], x2t[:, :, 0:T],
                                                ALU.subtract).then_inc(step_done, 1)
                    if slot == 1 and has(a):
                        wait(pool, ctx_hi_done, a)
                        wait(pool, v_ready, a - 1)
                        nc.gpsimd.tensor_tensor(ctx_lo[:], ctx_in[p][:], ctx_hi[:],
                                                ALU.subtract).then_inc(ctx_lo_done, 1)
                    if slot == 3 and has(b2):
                        wait(pool, res_loaded, b2, 16)
                        wait(pool, x2_done, b2 - 1)
                        nc.gpsimd.tensor_tensor(x_bias[:], x_res[:],
                                                bo_gated[:].unsqueeze(1).to_broadcast([P, C, D]),
                                                ALU.add).then_inc(bias_added, 1)
                    if slot == 4 and has(b3):
                        wait(pool, mk_hi_done, b3)
                        wait(pool, kf_ready, b3 - 1)
                        nc.gpsimd.tensor_tensor(mk_lo[:], mk[:], mk_hi[:],
                                                ALU.subtract).then_inc(mk_lo_done, 1)
                    if slot == 7 and has(b2):
                        rstd(var2, mv2, rstd2, mv2_done, var2_done, rstd2_done, x2n_done, b2)
                    if slot == 7 and has(b3):
                        wait(pool, y_done, b3)
                        wait(pool, stored, b3 - 1, 16)
                        nc.gpsimd.tensor_tensor(result[:], y[:], x2[1 - p][:],
                                                ALU.add).then_inc(result_done, 1)

            run(pool, iteration)


_INS = ['x', 'ctx_t', 'g_xattn', 'g_ffn', 'w_q', 'b_q', 'w_k', 'b_k', 'w_v', 'b_v', 'w_o', 'b_o',
        'w_r', 'w_kf', 'w_vf', 'mu_r', 'mu_k']


def kernel(x, ctx_1024, g_xattn, g_ffn, L0_xattn_Wq, L0_xattn_bq, L0_xattn_Wk, L0_xattn_bk,
           L0_xattn_Wv, L0_xattn_bv, L0_xattn_Wo, L0_xattn_bo, L0_ffn_W_r, L0_ffn_W_k, L0_ffn_W_v,
           L0_ffn_mu_r, L0_ffn_mu_k):
    import numpy as np
    import concourse.bacc as bacc
    from concourse import mybir
    from concourse.bass_utils import run_bass_kernel_spmd

    def columns(v):
        return np.asarray(v).reshape(2, 128).T

    def transposed(w):
        return np.swapaxes(np.asarray(w), -1, -2)

    laid_out = {
        'x': x, 'ctx_t': transposed(ctx_1024),
        'g_xattn': np.asarray(g_xattn).reshape(1, 1), 'g_ffn': np.asarray(g_ffn).reshape(1, 1),
        'w_q': transposed(L0_xattn_Wq), 'b_q': columns(L0_xattn_bq),
        'w_k': transposed(L0_xattn_Wk), 'b_k': columns(L0_xattn_bk),
        'w_v': transposed(L0_xattn_Wv), 'b_v': columns(L0_xattn_bv),
        'w_o': transposed(L0_xattn_Wo), 'b_o': np.asarray(L0_xattn_bo).reshape(1, 256),
        'w_r': transposed(L0_ffn_W_r), 'w_kf': transposed(L0_ffn_W_k),
        'w_vf': transposed(L0_ffn_W_v), 'mu_r': columns(L0_ffn_mu_r), 'mu_k': columns(L0_ffn_mu_k),
    }
    nc = bacc.Bacc("TRN2", target_bir_lowering=False, num_devices=1)
    arrays, args = {}, []
    for name in _INS:
        a = np.ascontiguousarray(laid_out[name])
        arrays[f"in_{name}"] = a
        args.append(nc.dram_tensor(f"in_{name}", a.shape, mybir.dt.from_np(a.dtype),
                                   kind="ExternalInput").ap())
    args.append(nc.dram_tensor("out_x", (16, 256, 256), mybir.dt.float32, kind="ExternalOutput").ap())
    flamingo_block(nc, *args)
    r = run_bass_kernel_spmd(nc, [arrays], core_ids=[0])
    return r.results[0]["out_x"]
```
